# Optimizing a Trainium2 kernel written in Bass

```python
import numpy as np
import jax
import jax.numpy as jnp

def _softmax(x, axis=-1):
    return jax.nn.softmax(x, axis=axis)

def _gelu(x):
    return jax.nn.gelu(x, approximate=True)

def _silu(x):
    return jax.nn.silu(x)

def _sigmoid(x):
    return jax.nn.sigmoid(x)

def _layernorm(x, axis=-1, eps=1e-05):
    m = jnp.mean(x, axis=axis, keepdims=True)
    v = jnp.var(x, axis=axis, keepdims=True)
    return (x - m) / jnp.sqrt(v + eps)

def _scatter_add(tgt, idx, src, axis=0):
    return tgt.at[idx].add(src)

def _segment_sum(src, seg, n):
    return jax.ops.segment_sum(src, seg, n)
kernel_name = 'mk_sandwich_d1_jaxref_r8_ac9704'

def setup_inputs(seed: int=0):
    np.random.seed(seed)
    _w = jnp.asarray

    def _L0_attn_setup():
        import jax, jax.numpy as jnp
        import numpy as np
        B, T, D = (4, 128, 128)
        H, DK, DV = (16, 32, 32)
        GAMMA = 0.99

        def _xavier(key, shape, gain=0.1):
            fan_in, fan_out = shape
            lim = gain * jnp.sqrt(6.0 / (fan_in + fan_out))
            return jax.random.uniform(key, shape, jnp.float32, -lim, lim)

        def _hla_forward(x, Wq, Wk, Wv, Wo):
            Bs, Ts, _ = x.shape
            q = (x @ Wq).reshape(Bs, Ts, H, DK).transpose(1, 0, 2, 3)
            k = (x @ Wk).reshape(Bs, Ts, H, DK).transpose(1, 0, 2, 3)
            v = (x @ Wv).reshape(Bs, Ts, H, DV).transpose(1, 0, 2, 3)
            S_K0 = jnp.zeros((Bs, H, DK, DK), x.dtype)
            C_QV0 = jnp.zeros((Bs, H, DK, DV), x.dtype)
            G0 = jnp.zeros((Bs, H, DK, DV), x.dtype)

            def step(carry, qkv):
                S_K, C_QV, G = carry
                q_t, k_t, v_t = qkv
                C_prev = GAMMA * C_QV
                k_C = jnp.einsum('bhk,bhkv->bhv', k_t, C_prev)
                G = GAMMA * G + k_t[..., :, None] * k_C[..., None, :]
                S_K = GAMMA * S_K + k_t[..., :, None] * k_t[..., None, :]
                C_QV = C_prev + q_t[..., :, None] * v_t[..., None, :]
                S_C = jnp.einsum('bhij,bhjv->bhiv', S_K, C_QV)
                o_t = jnp.einsum('bhk,bhkv->bhv', q_t, S_C - G)
                return ((S_K, C_QV, G), o_t)
            _, outs = jax.lax.scan(step, (S_K0, C_QV0, G0), (q, k, v))
            out = outs.transpose(1, 0, 2, 3).reshape(Bs, Ts, H * DV)
            return out @ Wo
        key = jax.random.key(seed)
        kx, kq, kk, kv, ko = jax.random.split(key, 5)
        return {'x': jax.random.normal(kx, (B, T, D), jnp.float32), 'Wq': _xavier(kq, (D, H * DK)), 'Wk': _xavier(kk, (D, H * DK)), 'Wv': _xavier(kv, (D, H * DV)), 'Wo': _xavier(ko, (H * DV, D))}
    _L0_attn_in = _L0_attn_setup()

    def _L0_ffn_setup():
        import jax, jax.numpy as jnp
        import numpy as np
        D_IN, D_HID = (128, 512)

        def _ternary(key, shape):
            return jax.random.randint(key, shape, -1, 2).astype(jnp.float32)

        def _tlin(x, w, s):
            return jnp.einsum('bsi,oi->bso', x, w) * s
        key = jax.random.key(seed)
        ks = jax.random.split(key, 12)
        inv = lambda fan: 1.0 / np.sqrt(fan).astype(np.float32)
        return {'x': jax.random.normal(ks[0], (4, 256, D_IN), dtype=jnp.float32), 'w1_w': _ternary(ks[1], (D_HID, D_IN)), 'w1_s': jax.random.uniform(ks[2], (D_HID,), dtype=jnp.float32) * inv(D_IN), 'w2_w': _ternary(ks[3], (D_HID, D_IN)), 'w2_s': jax.random.uniform(ks[4], (D_HID,), dtype=jnp.float32) * inv(D_IN), 'h1_w': _ternary(ks[5], (D_HID, D_HID)), 'h1_s': jax.random.uniform(ks[6], (D_HID,), dtype=jnp.float32) * inv(D_HID), 'h2_w': _ternary(ks[7], (D_HID, D_HID)), 'h2_s': jax.random.uniform(ks[8], (D_HID,), dtype=jnp.float32) * inv(D_HID), 'w3_w': _ternary(ks[9], (D_IN, D_HID)), 'w3_s': jax.random.uniform(ks[10], (D_IN,), dtype=jnp.float32) * inv(D_HID)}
    _L0_ffn_in = _L0_ffn_setup()
    _d = {'L0_attn_x': _L0_attn_in['x'], 'L0_attn_Wq': _L0_attn_in['Wq'], 'L0_attn_Wk': _L0_attn_in['Wk'], 'L0_attn_Wv': _L0_attn_in['Wv'], 'L0_attn_Wo': _L0_attn_in['Wo'], 'L0_ffn_w1_w': _L0_ffn_in['w1_w'], 'L0_ffn_w1_s': _L0_ffn_in['w1_s'], 'L0_ffn_w2_w': _L0_ffn_in['w2_w'], 'L0_ffn_w2_s': _L0_ffn_in['w2_s'], 'L0_ffn_h1_w': _L0_ffn_in['h1_w'], 'L0_ffn_h1_s': _L0_ffn_in['h1_s'], 'L0_ffn_h2_w': _L0_ffn_in['h2_w'], 'L0_ffn_h2_s': _L0_ffn_in['h2_s'], 'L0_ffn_w3_w': _L0_ffn_in['w3_w'], 'L0_ffn_w3_s': _L0_ffn_in['w3_s']}
    _x0 = _d['L0_attn_x']
    _d['L0_attn_x'] = jax.random.normal(jax.random.fold_in(jax.random.key(seed), 1), (16, 512, 128), dtype=_x0.dtype)
    del _x0
    return _d

def reference(L0_attn_x, L0_attn_Wq, L0_attn_Wk, L0_attn_Wv, L0_attn_Wo, L0_ffn_w1_w, L0_ffn_w1_s, L0_ffn_w2_w, L0_ffn_w2_s, L0_ffn_h1_w, L0_ffn_h1_s, L0_ffn_h2_w, L0_ffn_h2_s, L0_ffn_w3_w, L0_ffn_w3_s):

    def _L0_attn_ref(x, Wq, Wk, Wv, Wo):
        import jax, jax.numpy as jnp
        import numpy as np
        B, T, D = (4, 128, 128)
        H, DK, DV = (16, 32, 32)
        GAMMA = 0.99

        def _xavier(key, shape, gain=0.1):
            fan_in, fan_out = shape
            lim = gain * jnp.sqrt(6.0 / (fan_in + fan_out))
            return jax.random.uniform(key, shape, jnp.float32, -lim, lim)

        def _hla_forward(x, Wq, Wk, Wv, Wo):
            Bs, Ts, _ = x.shape
            q = (x @ Wq).reshape(Bs, Ts, H, DK).transpose(1, 0, 2, 3)
            k = (x @ Wk).reshape(Bs, Ts, H, DK).transpose(1, 0, 2, 3)
            v = (x @ Wv).reshape(Bs, Ts, H, DV).transpose(1, 0, 2, 3)
            S_K0 = jnp.zeros((Bs, H, DK, DK), x.dtype)
            C_QV0 = jnp.zeros((Bs, H, DK, DV), x.dtype)
            G0 = jnp.zeros((Bs, H, DK, DV), x.dtype)

            def step(carry, qkv):
                S_K, C_QV, G = carry
                q_t, k_t, v_t = qkv
                C_prev = GAMMA * C_QV
                k_C = jnp.einsum('bhk,bhkv->bhv', k_t, C_prev)
                G = GAMMA * G + k_t[..., :, None] * k_C[..., None, :]
                S_K = GAMMA * S_K + k_t[..., :, None] * k_t[..., None, :]
                C_QV = C_prev + q_t[..., :, None] * v_t[..., None, :]
                S_C = jnp.einsum('bhij,bhjv->bhiv', S_K, C_QV)
                o_t = jnp.einsum('bhk,bhkv->bhv', q_t, S_C - G)
                return ((S_K, C_QV, G), o_t)
            _, outs = jax.lax.scan(step, (S_K0, C_QV0, G0), (q, k, v))
            out = outs.transpose(1, 0, 2, 3).reshape(Bs, Ts, H * DV)
            return out @ Wo
        return _hla_forward(x, Wq, Wk, Wv, Wo)

    def _L0_ffn_ref(x, w1_w, w1_s, w2_w, w2_s, h1_w, h1_s, h2_w, h2_s, w3_w, w3_s):
        import jax, jax.numpy as jnp
        import numpy as np
        D_IN, D_HID = (128, 512)

        def _ternary(key, shape):
            return jax.random.randint(key, shape, -1, 2).astype(jnp.float32)

        def _tlin(x, w, s):
            return jnp.einsum('bsi,oi->bso', x, w) * s
        h = jax.nn.silu(_tlin(x, w1_w, w1_s)) * _tlin(x, w2_w, w2_s)
        h = jax.nn.gelu(_tlin(h, h1_w, h1_s), approximate=False)
        h = jax.nn.gelu(_tlin(h, h2_w, h2_s), approximate=False)
        return _tlin(h, w3_w, w3_s)
    x = L0_attn_x
    x = x + _layernorm(_L0_attn_ref(_layernorm(x, axis=-1), L0_attn_Wq, L0_attn_Wk, L0_attn_Wv, L0_attn_Wo), axis=-1)
    x = x + _layernorm(_L0_ffn_ref(_layernorm(x, axis=-1), L0_ffn_w1_w, L0_ffn_w1_s, L0_ffn_w2_w, L0_ffn_w2_s, L0_ffn_h1_w, L0_ffn_h1_s, L0_ffn_h2_w, L0_ffn_h2_s, L0_ffn_w3_w, L0_ffn_w3_s), axis=-1)
    return x

_drawn_inputs = setup_inputs


def setup_inputs(seed=0):
    import zlib

    import numpy as np

    out = dict(_drawn_inputs(seed))
    spreads = {}
    factors = {}
    for name, (base, spread) in spreads.items():
        noise = np.random.default_rng([zlib.crc32(name.encode()), seed]).standard_normal(out[name].shape)
        drawn = base * np.exp(spread * noise) if base else spread * noise
        out[name] = jnp.asarray(drawn.astype(out[name].dtype))
    for name, factor in factors.items():
        out[name] = (out[name] * factor).astype(out[name].dtype)
    return out
```

```python
from contextlib import ExitStack

import numpy as np

import concourse.bass as bass
from concourse import mybir

B, T, D = 16, 512, 128
H, DK = 16, 32
HID = 512
DECAY = 0.99
EPS = 1e-5
P = 128
NG = H // 4
NC = T // P
ITEMS = NG * NC
NU = NG * (NC - 1)
NM = HID // P

F32 = mybir.dt.float32
F32R = mybir.dt.float32r
ALU = mybir.AluOpType
ACT = mybir.ActivationFunctionType

NEWTON = 1
ROOT_STEPS = 2 + 5 * NEWTON

LOAD, LN1, XT, PROJ = -14, -12, -10, -8
LOAD_RES, WO, LN2A, LN2B, XT2, W12, H1, H2, W3, LN3 = 8, 19, 20, 21, 22, 23, 25, 29, 33, 34
FIRST_LOOPED, END_LOOPED = 3, B - 1
FIRST, END = -1, B + 2


def fills(slot):
    out = []
    for kind, off in (("w3", W3), ("wo", WO), ("xt2", XT2), ("xt", XT)):
        if off % ITEMS == slot:
            out.append((kind, 0, off))
    for kind, off in (("h1", H1), ("h2", H2)):
        for m in range(NM):
            if (off + m) % ITEMS == slot:
                out.append((kind, m, off + m))
    for m in range(NM):
        if (W12 + m // 2) % ITEMS == slot:
            out += [("gate", m, W12 + m // 2), ("up", m, W12 + m // 2)]
    for g in range(NG):
        off = PROJ + 4 * g
        for n, use in enumerate([("left", 2 * g), ("left", 2 * g + 1), ("kv", 2 * g), ("kv", 2 * g + 1)]):
            if (off + n // 2) % ITEMS == slot:
                out.append((*use, off + n // 2))
    return out


def mid_fills(slot):
    return fills(slot)[:(len(fills(slot)) + 1) // 2]


def end_fills(slot):
    return fills(slot)[(len(fills(slot)) + 1) // 2:]


RING = [(s, *use) for s in range(ITEMS) for use in fills(s)]
assert len(RING) % 2 == 0


def constants():
    k = DECAY ** -np.arange(T, dtype=np.float64)
    r, t = np.arange(P)[:, None], np.arange(P)[None, :]
    tri = (r <= t).astype(np.float64)
    p_mask = np.stack([tri / k[c * P:(c + 1) * P][None, :] for c in range(NC)], 1)
    d_mask = tri * (DECAY ** (t - r).astype(np.float64) - 1.0)
    quad = np.arange(P) // DK
    right_scale = np.tile(k[None, :], (P, 1))
    tok_kappa = k.reshape(NC, P).T
    eps_t = EPS * k.reshape(NC, P).T ** 4
    sk = np.zeros((P, 2, 2, DK))
    e = np.zeros((P, 2, DK))
    for row in range(P):
        h, part = quad[row] // 2, quad[row] % 2
        sk[row, h] = 1.0 if part == 0 else 0.0
        if part:
            sk[row, h, 0] = -1.0
        e[row, h] = 1.0
    out = {"c_tri": tri, "c_pmask": p_mask.reshape(P, NC * P), "c_dmask": d_mask,
           "c_rscale": right_scale, "c_kappa": tok_kappa, "c_eps": eps_t,
           "c_kappa1": np.stack([tok_kappa, np.ones((P, NC))], 2).reshape(P, -1),
           "c_small": np.tile(np.repeat([-0.5, 1.5, EPS, 1.0], NC), (P, 1)),
           "c_sk": sk.reshape(P, -1), "c_e": e.reshape(P, -1), "c_id": np.eye(P)}
    return {n: np.ascontiguousarray(a.astype(np.float32)) for n, a in out.items()}


def build(nc, x, w_left, w_kv, w_o, w_1, w_2, h_1, h_2, w_3, f_1, f_2, f_h1, f_h2, f_3, tables, out):
    with ExitStack() as ctx:
        def sb(name, shape, dt=F32):
            return ctx.enter_context(nc.sbuf_tensor(name, shape, dt))

        def bank(name):
            return ctx.enter_context(nc.psum_tensor(name, [P, 512], F32))

        def sem(name):
            return ctx.enter_context(nc.semaphore(name))

        def halves(name, n):
            return sb(name + "_hi", [P, n], F32R), sb(name + "_lo", [P, n], F32R)
        wl, wkv = halves("wl", 8 * P), halves("wkv", 2 * 512)
        w1, w2 = halves("w1", HID), halves("w2", HID)
        wh1, wh2 = halves("wh1", NM * HID), halves("wh2", NM * HID)
        wo = sb("wo", [P, NG, D])
        w3 = sb("w3", [P, NM, D])
        sc1, sc2, sch1, sch2 = (sb(n, [P, NM]) for n in ("sc1", "sc2", "sch1", "sch2"))

        tri, dmask = sb("tri", [P, P]), sb("dmask", [P, P])
        pmask = sb("pmask", [P, NC, P])
        rscale = sb("rscale", [P, T])
        kappa, eps_t = sb("kappa", [P, NC]), sb("eps_t", [P, NC])
        kappa1 = sb("kappa1", [P, NC, 2])
        skmask = sb("skmask", [P, 2, 2 * DK])
        emask = sb("emask", [P, 2, DK])
        ident = sb("ident", [P, P])
        small, held = sb("small", [P, 4, NC]), sb("held", [P, 1])

        xin, x2 = sb("xin", [P, NC, D]), sb("x2", [P, NC, D])
        xn2 = sb("xn2", [P, NC, D])
        stats, mv = sb("stats", [P, 4, NC, 6]), sb("mv", [P, 4, NC, 2])
        rstd, newton = sb("rstd", [P, 4, NC]), sb("newton", [P, 4, NC])
        xt, xt2 = halves("xt", T), halves("xt2", T)
        left, right = sb("left", [P, NG, 2, T]), sb("right", [P, NG, 2, T])
        kn, vn = sb("kn", [P, NG, NC, P]), sb("vn", [P, NG, NC, P])
        kk = sb("kk", [P, 2, 4, 2, DK])
        pm, dm, wt = sb("pm", [P, 2, 4, P]), sb("dm", [P, 2, 4, P]), sb("wt", [P, 2, 4, P])
        skbd = sb("skbd", [P, 2, 2, 2 * DK])
        ebd = sb("ebd", [P, 2, 2, DK])
        qpn = sb("qpn", [P, 2, 2, P])
        ot = sb("ot", [P, NG, T])
        silu = sb("silu", [P, HID])
        pre = sb("pre", [P, 2, T])
        hid, gel = halves("hid", NM * T), halves("gel", NM * T)
        gel2 = sb("gel2", [P, NM, T])
        outt = gel2[:, 0, :].rearrange("p (c d) -> p c d", c=NC)

        ps_aw = ctx.enter_context(nc.psum_tensor("ps_aw", [P, 2, 512], F32))
        ps_x, ps_o = bank("ps_x"), bank("ps_o")
        ps_sk, ps_e = bank("ps_sk"), bank("ps_e")
        ps_f = [bank("ps_f0"), bank("ps_f1")]
        aw_v = ps_aw[:].rearrange("p k (w r t) -> p w r k t", w=2, r=2)
        a_v, w_v = aw_v[:, 0], aw_v[:, 1]
        x_v = ps_x[:, 0:2 * P].rearrange("p (r t) -> p r t", r=2)
        t_v = ps_o[:, P:3 * P].rearrange("p (r t) -> p r t", r=2)
        sk_v = ps_sk[:, 0:4 * DK].rearrange("p (r f) -> p r f", r=2)
        e_v = ps_e[:, 0:2 * DK].rearrange("p (r f) -> p r f", r=2)
        f_v = [b[:].rearrange("p (c d) -> p c d", c=4) for b in ps_f]

        s_raw, s_const, s_split, s_consts = sem("raw_loaded"), sem("const_loaded"), sem("weights_split"), sem("hi_written")
        s_x, s_xr, s_out = sem("x_loaded"), sem("xres_loaded"), sem("out_stored")
        s_ln = [sem(f"ln{i}_step") for i in range(4)]
        s_xt, s_xhi, s_xlo = sem("xt_ready"), sem("xt_hi"), sem("xt_lo")
        s_xt2, s_x2hi, s_x2lo = sem("xt2_ready"), sem("xt2_hi"), sem("xt2_lo")
        s_left, s_kv = sem("left_ready"), sem("kv_ready")
        s_leftc, s_rightc, s_kn, s_vn = sem("left_copied"), sem("right_copied"), sem("k_copied"), sem("v_copied")
        s_kk = sem("kappa_k")
        s_a, s_m = sem("scores_ready"), sem("scores_masked")
        s_xr_, s_p, s_d = sem("pd_ready"), sem("p_copied"), sem("d_copied")
        s_sk, s_skbd = sem("sk_ready"), sem("sk_spread")
        s_t, s_qpn = sem("qp_turned"), sem("qp_copied")
        s_w, s_wt = sem("weights_ready"), sem("weights_masked")
        s_o, s_ot = sem("o_ready"), sem("o_copied")
        s_e, s_ebd = sem("e_ready"), sem("e_spread")
        s_y, s_x2 = sem("y_ready"), sem("x2_added")
        s_gate, s_up, s_silu, s_h = sem("gate_ready"), sem("up_ready"), sem("silu_done"), sem("h_done")
        s_hhi, s_hlo = sem("pre_hi"), sem("pre_lo")
        s_h1, s_g1, s_h2, s_g2 = sem("h1_ready"), sem("gelu1_done"), sem("h2_ready"), sem("gelu2_done")
        s_w3, s_fin = sem("w3_ready"), sem("out_added")
        s_yc, s_w3c = sem("y_copied"), sem("w3_copied")
        s_root = [sem(f"ln{i}_root_step") for i in range(4)]

        def count(bb, per, index):
            return bb * per + (index + 1)

        def due(n):
            return not isinstance(n, int) or n > 0

        def has(it, off):
            return not isinstance(it, int) or 0 <= it - off // ITEMS < B

        def batch(it, off):
            return it - off // ITEMS

        def items(it, slot, lag):
            j = slot - lag
            bb = it if j >= 0 else it - 1
            if isinstance(bb, int) and not 0 <= bb < B:
                return None
            j %= ITEMS
            return bb, j, j // NC, j % NC

        def runs(eng, body):
            for it in range(FIRST, FIRST_LOOPED):
                body(it)
            with eng.Fori(FIRST_LOOPED, END_LOOPED) as it:
                body(it)
            for it in range(END_LOOPED, END):
                body(it)

        def freed_by(kind, n):
            return {
                "xt": [(s_xhi, 1, 0), (s_xlo, 1, 0)],
                "xt2": [(s_x2hi, 1, 0), (s_x2lo, 1, 0)],
                "left": [(s_rightc, 8, n)],
                "kv": [(s_kn, 8, n), (s_vn, 8, n)],
                "wo": [(s_yc, 1, 0)], "w3": [(s_w3c, 1, 0)],
                "gate": [(s_silu, 4, n)], "up": [(s_h, 4, n)],
                "h1": [(s_g1, 4, n)], "h2": [(s_g2, 4, n)],
            }[kind]

        def ring_place(kind, n):
            return next(i for i, u in enumerate(RING) if u[1:3] == (kind, n))

        def fill_bank(kind, n):
            return ring_place(kind, n) % 2

        def wait_bank_free(pe, it, kind, n):
            i = ring_place(kind, n)
            for back in range(2, 3 * len(RING), 2):
                turn, at = divmod(i - back, len(RING))
                _, pkind, pn, poff = RING[at]
                pit = it + turn
                if isinstance(pit, int) and not 0 <= pit - poff // ITEMS < B:
                    if pit < FIRST:
                        return
                    continue
                for s, per, index in freed_by(pkind, pn):
                    pe.wait_ge(s, count(batch(pit, poff), per, index))
                return

        NCONST = 11 + 4 + 3
        block = ctx.enter_context(nc.Block())

        raw_names = [("left", w_left, wl, 8 * P), ("kv", w_kv, wkv, 2 * 512), ("1", w_1, w1, HID), ("2", w_2, w2, HID)] + [
            (f"h1{k}", h_1[:, k * HID:(k + 1) * HID], (wh1[0][:, k * HID:(k + 1) * HID], wh1[1][:, k * HID:(k + 1) * HID]), HID) for k in range(NM)] + [
            (f"h2{k}", h_2[:, k * HID:(k + 1) * HID], (wh2[0][:, k * HID:(k + 1) * HID], wh2[1][:, k * HID:(k + 1) * HID]), HID) for k in range(NM)]
        stage = [left[:, 0].rearrange("p a b -> p (a b)"), left[:, 1].rearrange("p a b -> p (a b)"),
                 left[:, 2].rearrange("p a b -> p (a b)")[:, 0:512], left[:, 2].rearrange("p a b -> p (a b)")[:, 512:1024],
                 left[:, 3].rearrange("p a b -> p (a b)")[:, 0:512], left[:, 3].rearrange("p a b -> p (a b)")[:, 512:1024],
                 right[:, 0].rearrange("p a b -> p (a b)")[:, 0:512], right[:, 0].rearrange("p a b -> p (a b)")[:, 512:1024],
                 right[:, 1].rearrange("p a b -> p (a b)")[:, 0:512], right[:, 1].rearrange("p a b -> p (a b)")[:, 512:1024],
                 right[:, 2].rearrange("p a b -> p (a b)")[:, 0:512], right[:, 2].rearrange("p a b -> p (a b)")[:, 512:1024]]
        raw3 = right[:, 3, 0, :].rearrange("p (m d) -> p m d", m=NM)
        row3 = right[:, 3, 1, 0:D]
        NSTAGE = len(stage)

        @block.sync
        def _(sp):
            consts = [(tri[:], "c_tri"), (dmask[:], "c_dmask"), (pmask[:].rearrange("p c t -> p (c t)"), "c_pmask"),
                      (rscale[:], "c_rscale"), (kappa[:], "c_kappa"), (eps_t[:], "c_eps"),
                      (skmask[:].rearrange("p a b -> p (a b)"), "c_sk"), (emask[:].rearrange("p a b -> p (a b)"), "c_e"),
                      (ident[:], "c_id"), (small[:].rearrange("p a b -> p (a b)"), "c_small"),
                      (kappa1[:].rearrange("p a b -> p (a b)"), "c_kappa1")]

            def load(it):
                if has(it, LOAD):
                    bb = batch(it, LOAD)
                    if due(seen := count(bb, 1, -1)):
                        sp.wait_ge(s_xt, seen)
                    sp.dma_start(xin[:], x[bb].rearrange("(c p) d -> p c d", p=P)).then_inc(s_x, 16)

            def body(it):
                for slot in range(ITEMS):
                    if slot == LOAD % ITEMS and it is not FIRST:
                        load(it)
                    if slot == LOAD_RES % ITEMS and has(it, LOAD_RES):
                        bb = batch(it, LOAD_RES)
                        if due(seen := count(bb, 1, -1)):
                            sp.wait_ge(s_xt2, seen)
                        sp.dma_start(xn2[:], x[bb].rearrange("(c p) d -> p c d", p=P)).then_inc(s_xr, 16)
                    if slot == LN3 % ITEMS and has(it, LN3):
                        bb = batch(it, LN3)
                        sp.wait_ge(s_fin, count(bb, 1, 0))
                        sp.dma_start(out[bb].rearrange("(c p) d -> p c d", p=P), outt).then_inc(s_out, 16)
            load(FIRST)
            for n, (dst, name) in enumerate(consts):
                sp.dma_start(dst, tables[name]).then_inc(s_const, 16)
            for dst, src in ((sc1, f_1), (sc2, f_2), (sch1, f_h1), (sch2, f_h2)):
                sp.dma_start(dst[:], src).then_inc(s_const, 16)
            sp.dma_start(wo[:], w_o.rearrange("(g p) d -> p g d", p=P)).then_inc(s_const, 16)
            sp.dma_start(raw3, w_3.rearrange("(m p) d -> p m d", p=P)).then_inc(s_const, 16)
            sp.dma_start(row3, f_3).then_inc(s_const, 16)
            for n, (_, src, _, _) in enumerate(raw_names):
                sp.dma_start(stage[n], src).then_inc(s_raw, 16)
            runs(sp, body)
            sp.wait_ge(s_out, 16 * B)
        @block.tensor
        def _(pe):
            mm = nc.tensor.matmul

            def three(dst, lo_hi_l, lo_hi_r, start=True, stop=True):
                (lh, ll), (rh, rl) = lo_hi_l, lo_hi_r
                mm(dst, ll, rh, start=start, stop=False)
                mm(dst, lh, rl, start=False, stop=False)
                return mm(dst, lh, rh, start=False, stop=stop)

            def scores(bb, j, g, c):
                n = count(bb, ITEMS, j)
                if c == 0:
                    pe.wait_ge(s_leftc, count(bb, 8, 2 * g + 1))
                    pe.wait_ge(s_rightc, count(bb, 8, 2 * g + 1))
                if due(seen := n - 1):
                    pe.wait_ge(s_m, seen)
                if due(seen := n - 3):
                    pe.wait_ge(s_wt, seen)
                for h in range(4):
                    r, q = h // 2, 64 * (h % 2) + DK
                    m = mm(a_v[:, r, h % 2, :], left[q:q + DK, g, r, c * P:(c + 1) * P],
                           right[q:q + DK, g, r, c * P:(c + 1) * P], start=True, stop=True)
                m.then_inc(s_a, 1)

            def pd(bb, j, g, c):
                n, b2 = count(bb, ITEMS, j), j % 2
                if c == 0:
                    pe.wait_ge(s_kn, count(bb, 8, 2 * g + 1))
                else:
                    if due(seen := count(bb, NU, 3 * g + c - 1)):
                        pe.wait_ge(s_skbd, seen)
                pe.wait_ge(s_m, n)
                if due(seen := n - 1):
                    pe.wait_ge(s_p, seen)
                if due(seen := n - 1):
                    pe.wait_ge(s_d, seen)
                for r in range(2):
                    if c:
                        mm(x_v[:, r, :], skbd[:, r].rearrange("p a b -> p (a b)"), right[:, g, r, c * P:(c + 1) * P],
                           start=True, stop=False, skip_group_check=True)
                    for part, src in ((0, dm), (1, pm)):
                        for hh in range(2):
                            q, h = 64 * hh + DK * part, 2 * r + hh
                            m = mm(x_v[q:q + DK, r, :], kn[:, g, c, h * DK:(h + 1) * DK], src[:, b2, h, :],
                                   start=(c == 0), stop=True, skip_group_check=True)
                m.then_inc(s_xr_, 1)

            def update_sk(bb, j, g, c):
                u = 3 * g + c
                pe.wait_ge(s_kk, count(bb, NU, u))
                if due(seen := count(bb, NU, u - 1)):
                    pe.wait_ge(s_skbd, seen)
                for r in range(2):
                    for hh in range(2):
                        h, q = 2 * r + hh, 64 * hh
                        kh = kn[:, g, c, h * DK:(h + 1) * DK]
                        mm(sk_v[q:q + DK, r, :], kh, kk[:, u % 2, h].rearrange("p a b -> p (a b)"),
                           start=(c == 0 and r == 0), stop=True, skip_group_check=True)
                        m = mm(sk_v[q + DK:q + 2 * DK, r, 0:DK], kh, kh, start=(c == 0 and r == 0), stop=True,
                               skip_group_check=True)
                m.then_inc(s_sk, 1)

            def turn_qp(bb, j, g, c):
                u = 3 * g + c
                pe.wait_ge(s_p, count(bb, ITEMS, j))
                if due(seen := count(bb, NU, u - 1)):
                    pe.wait_ge(s_qpn, seen)
                if due(seen := count(bb, ITEMS, j) - 2):
                    pe.wait_ge(s_ot, seen)
                for r in range(2):
                    m = nc.tensor.transpose(t_v[:, r, :], left[:, g, r, c * P:(c + 1) * P], ident[:])
                m.then_inc(s_t, 1)

            def weights(bb, j, g, c, newest):
                n = count(bb, ITEMS, j)
                if newest:
                    pe.wait_ge(s_m, count(newest[0], ITEMS, newest[1]))
                pe.wait_ge(s_p, n)
                pe.wait_ge(s_d, n)
                if due(seen := n - 1):
                    pe.wait_ge(s_wt, seen)
                for h in range(4):
                    r, q = h // 2, 64 * (h % 2)
                    m = mm(w_v[:, r, h % 2, :], left[q:q + 64, g, r, c * P:(c + 1) * P],
                           right[q:q + 64, g, r, c * P:(c + 1) * P], start=True, stop=True)
                m.then_inc(s_w, 1)

            def outputs(bb, j, g, c):
                n, b2 = count(bb, ITEMS, j), j % 2
                if c == 0:
                    pe.wait_ge(s_vn, count(bb, 8, 2 * g + 1))
                else:
                    if due(seen := count(bb, NU, 3 * g + c - 1)):
                        pe.wait_ge(s_ebd, seen)
                pe.wait_ge(s_wt, n)
                if due(seen := n - 1):
                    pe.wait_ge(s_ot, seen)
                if c:
                    for r in range(2):
                        mm(ps_o[64 * r:64 * r + 64, 0:P], ebd[:, r].rearrange("p a b -> p (a b)"),
                           right[:, g, r, c * P:(c + 1) * P], start=True, stop=False, skip_group_check=True)
                for h in range(4):
                    m = mm(ps_o[DK * h:DK * h + DK, 0:P], vn[:, g, c, h * DK:(h + 1) * DK], wt[:, b2, h, :],
                           start=(c == 0), stop=True, skip_group_check=True)
                m.then_inc(s_o, 1)

            def update_e(bb, j, g, c):
                u = 3 * g + c
                pe.wait_ge(s_qpn, count(bb, NU, u))
                if due(seen := count(bb, NU, u - 1)):
                    pe.wait_ge(s_ebd, seen)
                for r in range(2):
                    for hh in range(2):
                        h = 2 * r + hh
                        m = mm(e_v[64 * hh:64 * hh + 64, r, :], qpn[:, u % 2, r, 64 * hh:64 * hh + 64],
                               vn[:, g, c, h * DK:(h + 1) * DK], start=(c == 0 and r == 0), stop=True,
                               skip_group_check=True)
                m.then_inc(s_e, 1)

            def cols(pair, a, b):
                return pair[0][:, a:b], pair[1][:, a:b]

            def fill(it, kind, n, off):
                bb = batch(it, off)
                wait_bank_free(pe, it, kind, n)
                f = fill_bank(kind, n)
                dst = ps_f[f]
                if kind in ("xt", "xt2"):
                    src, s, t = (xin, s_ln[0], s_xt) if kind == "xt" else (xn2, s_ln[2], s_xt2)
                    pe.wait_ge(s, count(bb, 3, 2))
                    for c in range(NC):
                        m = nc.tensor.transpose(f_v[f][:, c, :], src[:, c, :], ident[:])
                    m.then_inc(t, 1)
                elif kind == "left":
                    pe.wait_ge(s_xlo, count(bb, 1, 0))
                    three(dst[:], cols(wl, n * P, (n + 1) * P), (xt[0][:], xt[1][:])).then_inc(s_left, 1)
                elif kind == "kv":
                    pe.wait_ge(s_xlo, count(bb, 1, 0))
                    g = n // 2
                    for i in range(2):
                        c = 2 * (n % 2) + i
                        m = three(dst[:, 256 * i:256 * i + 256], cols(xt, c * P, (c + 1) * P), cols(wkv, 256 * g, 256 * g + 256))
                    m.then_inc(s_kv, 1)
                elif kind == "wo":
                    if due(seen := count(bb, ITEMS, ITEMS - 1)):
                        pe.wait_ge(s_ot, seen)
                    for c in range(NC):
                        for g in range(NG):
                            m = mm(f_v[f][:, c, :], ot[:, g, c * P:(c + 1) * P], wo[:, g, :], start=(g == 0), stop=(g == NG - 1))
                    m.then_inc(s_y, 1)
                elif kind in ("gate", "up"):
                    pe.wait_ge(s_x2lo, count(bb, 1, 0))
                    w, s = (w1, s_gate) if kind == "gate" else (w2, s_up)
                    three(dst[:], cols(w, n * P, (n + 1) * P), (xt2[0][:], xt2[1][:])).then_inc(s, 1)
                elif kind in ("h1", "h2"):
                    w, src, s = (wh1, hid, s_h1) if kind == "h1" else (wh2, gel, s_h2)
                    for k in range(NM):
                        if n == 0:
                            pe.wait_ge(s_hlo, count(bb, 8, k + (4 if kind == "h2" else 0)))
                        m = three(dst[:], cols(w, k * HID + n * P, k * HID + (n + 1) * P), cols(src, k * T, (k + 1) * T),
                                  start=(k == 0), stop=(k == NM - 1))
                    m.then_inc(s, 1)
                elif kind == "w3":
                    pe.wait_ge(s_g2, count(bb, 4, 3))
                    for c in range(NC):
                        for k in range(NM):
                            m = mm(f_v[f][:, c, :], gel2[:, k, c * P:(c + 1) * P], w3[:, k, :], start=(k == 0), stop=(k == NM - 1))
                    m.then_inc(s_w3, 1)

            def body(it):
                for slot in range(ITEMS):
                    i0, i1, i2, i3 = (items(it, slot, lag) for lag in range(4))
                    if i0:
                        scores(*i0)
                    if i1:
                        pd(*i1)
                        if i1[3] < NC - 1:
                            update_sk(*i1)
                    for kind, n, off in mid_fills(slot):
                        if has(it, off):
                            fill(it, kind, n, off)
                    if i2:
                        if i2[3] < NC - 1:
                            turn_qp(*i2)
                        weights(*i2, i0)
                    if i3:
                        if i2 and i2[3] < NC - 1:
                            pe.wait_ge(s_qpn, count(i2[0], NU, 3 * i2[2] + i2[3]))
                        outputs(*i3)
                        if i3[3] < NC - 1:
                            update_e(*i3)
                    for kind, n, off in end_fills(slot):
                        if has(it, off):
                            fill(it, kind, n, off)

            pe.wait_ge(s_const, 16 * NCONST)
            pe.wait_ge(s_split, 2 * NSTAGE + 1)
            runs(pe, body)

        @block.scalar
        def _(act):
            fn = nc.scalar.activation

            def body(it):
                for slot in range(ITEMS):
                    i1, i2, i3 = (items(it, slot, lag) for lag in (1, 2, 3))
                    if i1:
                        bb, j, g, c = i1
                        act.wait_ge(s_xr_, count(bb, ITEMS, j))
                        for hh in range(2):
                            q = 64 * hh + DK
                            m = fn(left[q:q + DK, g, :, c * P:(c + 1) * P], x_v[q:q + DK, :, :], ACT.Copy)
                        m.then_inc(s_p, 1)
                    for kind, n, off in mid_fills(slot):
                        if has(it, off):
                            fill(it, kind, n, off)
                    if i2 and i2[3] < NC - 1:
                        bb, j, g, c = i2
                        u = 3 * g + c
                        act.wait_ge(s_t, count(bb, NU, u))
                        if due(seen := count(bb, NU, u - 2)):
                            act.wait_ge(s_e, seen)
                        fn(qpn[:, u % 2], t_v[:, :, :], ACT.Copy).then_inc(s_qpn, 1)
                    if i3:
                        bb, j, g, c = i3
                        act.wait_ge(s_o, count(bb, ITEMS, j))
                        if c == 0:
                            if due(seen := count(bb, 1, -1)):
                                act.wait_ge(s_y, seen)
                        fn(ot[:, g, c * P:(c + 1) * P], ps_o[:, 0:P], ACT.Copy).then_inc(s_ot, 1)
                    for kind, n, off in end_fills(slot):
                        if has(it, off):
                            fill(it, kind, n, off)

            def fill(it, kind, n, off):
                bb = batch(it, off)
                f = fill_bank(kind, n)
                src = ps_f[f][:]
                if kind == "xt":
                    act.wait_ge(s_xt, count(bb, 1, 0))
                    if due(seen := count(bb, 8, -1)):
                        act.wait_ge(s_kv, seen)
                    if due(seen := count(bb, 1, -1)):
                        act.wait_ge(s_xlo, seen)
                    fn(xt[0][:], src, ACT.Copy).then_inc(s_xhi, 1)
                elif kind == "xt2":
                    act.wait_ge(s_xt2, count(bb, 1, 0))
                    if due(seen := count(bb, 4, -1)):
                        act.wait_ge(s_up, seen)
                    if due(seen := count(bb, 1, -1)):
                        act.wait_ge(s_x2lo, seen)
                    fn(xt2[0][:], src, ACT.Copy).then_inc(s_x2hi, 1)
                elif kind == "left":
                    g = n // 2
                    act.wait_ge(s_left, count(bb, 8, n))
                    if due(seen := count(bb, ITEMS, 4 * g + 3 - ITEMS)):
                        act.wait_ge(s_w, seen)
                    fn(left[:, g, n % 2, :], src, ACT.Copy)
                    if due(seen := count(bb, ITEMS, 4 * g + 3 - ITEMS)):
                        act.wait_ge(s_o, seen)
                    fn(right[:, g, n % 2, :], src, ACT.Copy).then_inc(s_leftc, 1)
                elif kind == "wo":
                    act.wait_ge(s_y, count(bb, 1, 0))
                    if due(seen := count(bb, 1, -1)):
                        act.wait_ge(s_fin, seen)
                    fn(x2[:].rearrange("p c d -> p (c d)"), src, ACT.Copy).then_inc(s_yc, 1)
                elif kind == "w3":
                    act.wait_ge(s_w3, count(bb, 1, 0))
                    fn(gel2[:, 0, :], src, ACT.Copy).then_inc(s_w3c, 1)
                elif kind == "kv":
                    g = n // 2
                    act.wait_ge(s_kv, count(bb, 8, n))
                    if due(seen := count(bb, ITEMS, 4 * g + 3 - ITEMS)):
                        act.wait_ge(s_xr_, seen)
                    v = src.rearrange("p (i k d) -> p i k d", i=2, k=2)
                    c = 2 * (n % 2)
                    fn(kn[:, g, c:c + 2, :], v[:, :, 0, :], ACT.Copy).then_inc(s_kn, 1)
                elif kind == "gate":
                    act.wait_ge(s_gate, count(bb, 4, n))
                    if due(seen := count(bb, 4, n - 1)):
                        act.wait_ge(s_h, seen)
                    fn(silu[:], src, ACT.Silu, scale=sc1[:, n:n + 1]).then_inc(s_silu, 1)
                elif kind == "h1":
                    act.wait_ge(s_h1, count(bb, 4, n))
                    if due(seen := count(bb, 8, 4 + n - 2)):
                        act.wait_ge(s_hlo, seen)
                    fn(pre[:, n % 2, :], src, ACT.Gelu, scale=sch1[:, n:n + 1]).then_inc(s_g1, 1)
                elif kind == "h2":
                    act.wait_ge(s_h2, count(bb, 4, n))
                    if due(seen := 16 * count(bb, 1, -1)):
                        act.wait_ge(s_out, seen)
                    fn(gel2[:, n, :], src, ACT.Gelu, scale=sch2[:, n:n + 1]).then_inc(s_g2, 1)

            act.wait_ge(s_raw, 16 * NSTAGE)
            act.wait_ge(s_const, 16 * NCONST)
            for n, (_, _, (hi, lo), _) in enumerate(raw_names):
                fn(hi[:], stage[n], ACT.Copy).then_inc(s_consts, 1)
            act.wait_ge(s_split, 2 * NSTAGE + 1)
            runs(act, body)

        @block.vector
        def _(dve):
            tt, ts = nc.vector.tensor_tensor, nc.vector.tensor_scalar

            def per_head(m):
                return m.unsqueeze(1).unsqueeze(1).to_broadcast([P, 2, 2, P])

            def pairs(tile):
                return tile.rearrange("p (r k) t -> p r k t", r=2)

            LNS = (("ln1", LN1, s_x, 16, xin, xin), ("ln2a", LN2A, s_yc, 1, x2, x2), ("ln2b", LN2B, s_x2, 1, x2, xn2),
                   ("ln3", LN3, s_w3c, 1, outt, outt))

            def moments(which, bb):
                s, (_, _, made, step, src, _) = s_ln[which], LNS[which]
                dve.wait_ge(made, step * count(bb, 1, 0))
                for c in range(NC):
                    m = nc.vector.bn_stats(stats[:, which, c, :], src[:, c, :])
                m.then_inc(s, 1)
                dve.wait_ge(s, count(bb, 3, 0))
                nc.vector.tensor_copy(held[:], small[:, 0, 0:1])
                for c in range(NC):
                    m = nc.vector.bn_aggr(mv[:, which, c, :], stats[:, which, c, :])
                m.then_inc(s, 1)

            def normalise(which, bb):
                s, (_, _, _, _, src, dst) = s_ln[which], LNS[which]
                dve.wait_ge(s_root[which], count(bb, ROOT_STEPS, ROOT_STEPS - 1))
                for c in range(NC):
                    m = ts(dst[:, c, :], src[:, c, :], mv[:, which, c, 0:1], rstd[:, which, c:c + 1], ALU.subtract, ALU.mult)
                m.then_inc(s, 1)

            def body(it):
                for slot in range(ITEMS):
                    i0, i1, i2, i3 = (items(it, slot, lag) for lag in range(4))
                    if i0:
                        bb, j, g, c = i0
                        n = count(bb, ITEMS, j)
                        dve.wait_ge(s_a, n)
                        if due(seen := n - 2):
                            dve.wait_ge(s_xr_, seen)
                        tt(pairs(pm[:, j % 2]), a_v, per_head(pmask[:, c, :]), ALU.mult)
                        tt(pairs(dm[:, j % 2]), a_v, per_head(dmask[:]), ALU.mult).then_inc(s_m, 1)
                    if i1:
                        bb, j, g, c = i1
                        dve.wait_ge(s_xr_, count(bb, ITEMS, j))
                        for hh in range(2):
                            q = 64 * hh
                            m = nc.vector.tensor_copy(right[q:q + DK, g, :, c * P:(c + 1) * P], x_v[q:q + DK, :, :])
                        m.then_inc(s_d, 1)
                        if c < NC - 1:
                            dve.wait_ge(s_sk, count(bb, NU, 3 * g + c))
                            for r in range(2):
                                m = tt(skbd[:, r], sk_v[:, r, :].unsqueeze(1).to_broadcast([P, 2, 2 * DK]), skmask[:], ALU.mult)
                            m.then_inc(s_skbd, 1)
                    for which, (_, off, *_) in enumerate(LNS):
                        if slot == off % ITEMS and has(it, off):
                            moments(which, batch(it, off))
                    for kind, n, off in mid_fills(slot):
                        if has(it, off):
                            fill(it, kind, n, off)
                    if i2:
                        bb, j, g, c = i2
                        n = count(bb, ITEMS, j)
                        dve.wait_ge(s_w, n)
                        if due(seen := n - 2):
                            dve.wait_ge(s_o, seen)
                        tt(pairs(wt[:, j % 2]), w_v, per_head(tri[:]), ALU.mult).then_inc(s_wt, 1)
                    if i3 and i3[3] < NC - 1:
                        bb, j, g, c = i3
                        dve.wait_ge(s_e, count(bb, NU, 3 * g + c))
                        for r in range(2):
                            m = tt(ebd[:, r], e_v[:, r, :].unsqueeze(1).to_broadcast([P, 2, DK]), emask[:], ALU.mult)
                        m.then_inc(s_ebd, 1)
                    for which, (_, off, *_) in enumerate(LNS):
                        if slot == off % ITEMS and has(it, off):
                            normalise(which, batch(it, off))
                    for kind, n, off in end_fills(slot):
                        if has(it, off):
                            fill(it, kind, n, off)

            def fill(it, kind, n, off):
                bb = batch(it, off)
                f = fill_bank(kind, n)
                src = ps_f[f][:]
                if kind in ("xt", "xt2"):
                    hi, lo = xt if kind == "xt" else xt2
                    dve.wait_ge(s_xhi if kind == "xt" else s_x2hi, count(bb, 1, 0))
                    tt(lo[:], src, hi[:].bitcast(F32), ALU.subtract).then_inc(s_xlo if kind == "xt" else s_x2lo, 1)
                elif kind == "left":
                    g = n // 2
                    dve.wait_ge(s_leftc, count(bb, 8, n))
                    for hh in range(2):
                        q = 64 * hh
                        m = tt(right[q + DK:q + 2 * DK, g, n % 2, :], ps_f[f][q:q + DK, :], rscale[q:q + DK, :], ALU.mult)
                    m.then_inc(s_rightc, 1)
                elif kind == "kv":
                    g = n // 2
                    dve.wait_ge(s_kn, count(bb, 8, n))
                    if due(seen := count(bb, ITEMS, 4 * g + 3 - ITEMS)):
                        dve.wait_ge(s_o, seen)
                    v = src.rearrange("p (i k d) -> p i k d", i=2, k=2)
                    c = 2 * (n % 2)
                    tt(vn[:, g, c:c + 2, :], v[:, :, 1, :], kappa[:, c:c + 2].unsqueeze(2).to_broadcast([P, 2, P]),
                       ALU.mult).then_inc(s_vn, 1)
                elif kind == "up":
                    dve.wait_ge(s_up, count(bb, 4, n))
                    dve.wait_ge(s_silu, count(bb, 4, n))
                    if due(seen := count(bb, 8, n - 2)):
                        dve.wait_ge(s_hlo, seen)
                    nc.vector.scalar_tensor_tensor(out=pre[:, n % 2, :], in0=src, scalar=sc2[:, n:n + 1], in1=silu[:],
                                                   op0=ALU.mult, op1=ALU.mult).then_inc(s_h, 1)

            nc.vector.memset(ps_sk[:], 0.0)
            dve.wait_ge(s_raw, 16 * NSTAGE)
            for n, (_, _, (hi, lo), _) in enumerate(raw_names):
                dve.wait_ge(s_consts, n + 1)
                tt(lo[:], stage[n], hi[:].bitcast(F32), ALU.subtract).then_inc(s_split, 2)
            dve.wait_ge(s_const, 16 * NCONST)
            tt(w3[:], raw3, row3.unsqueeze(1).to_broadcast([P, NM, D]), ALU.mult).then_inc(s_split, 1)
            dve.wait_ge(s_split, 2 * NSTAGE + 1)
            runs(dve, body)

        @block.gpsimd
        def _(pool):
            tt = nc.gpsimd.tensor_tensor

            def root(which, bb):
                s, step = s_root[which], iter(range(ROOT_STEPS))
                v, y, z = mv[:, which, :, 1], rstd[:, which, :], newton[:, which, :]
                pool.wait_ge(s_ln[which], count(bb, 3, 1))

                def then(ins):
                    i = next(step)
                    ins.then_inc(s, 1)
                    if i < ROOT_STEPS - 1:
                        pool.wait_ge(s, count(bb, ROOT_STEPS, i))
                minus_half, three_halves, eps = (small[:, i, :] for i in range(3))
                then(tt(v, v, eps_t[:] if which == 1 else eps, ALU.add))
                then(tt(y, v, minus_half, ALU.pow))
                for _ in range(NEWTON):
                    then(tt(z, y, y, ALU.mult))
                    then(tt(z, z, v, ALU.mult))
                    then(tt(z, z, minus_half, ALU.mult))
                    then(tt(z, z, three_halves, ALU.add))
                    then(tt(y, y, z, ALU.mult))

            def body(it):
                for slot in range(ITEMS):
                    i0 = items(it, slot, 0)
                    if i0 and i0[3] < NC - 1:
                        bb, j, g, c = i0
                        u = 3 * g + c
                        pool.wait_ge(s_kn, count(bb, 8, 2 * g + c // 2))
                        if due(seen := count(bb, NU, u - 2)):
                            pool.wait_ge(s_sk, seen)
                        tt(kk[:, u % 2], kn[:, g, c, :].rearrange("p (h d) -> p h d", h=4).unsqueeze(2).to_broadcast([P, 4, 2, DK]),
                           kappa1[:, c, :].unsqueeze(1).unsqueeze(3).to_broadcast([P, 4, 2, DK]), ALU.mult).then_inc(s_kk, 1)
                    for which, off in enumerate((LN1, LN2A, LN2B, LN3)):
                        if slot == off % ITEMS and has(it, off):
                            root(which, batch(it, off))
                    if slot == LN2A % ITEMS and has(it, LN2A):
                        bb = batch(it, LN2A)
                        pool.wait_ge(s_ln[1], count(bb, 3, 2))
                        pool.wait_ge(s_xr, 16 * count(bb, 1, 0))
                        tt(x2[:], x2[:], xn2[:], ALU.add).then_inc(s_x2, 1)
                    if slot == LN3 % ITEMS and has(it, LN3):
                        bb = batch(it, LN3)
                        pool.wait_ge(s_ln[3], count(bb, 3, 2))
                        tt(outt, outt, x2[:], ALU.add).then_inc(s_fin, 1)
                    for kind, n, off in fills(slot):
                        if kind in ("up", "h1") and has(it, off):
                            bb = batch(it, off)
                            i = n + (4 if kind == "h1" else 0)
                            (hi, lo), made, used = (hid, s_h, s_h1) if kind == "up" else (gel, s_g1, s_h2)
                            hi, lo = (y[:, n * T:(n + 1) * T] for y in (hi, lo))
                            pool.wait_ge(made, count(bb, 4, n))
                            if due(seen := count(bb, 4, -1)):
                                pool.wait_ge(used, seen)
                            if due(seen := count(bb, 8, i - 8)):
                                pool.wait_ge(s_hlo, seen)
                            tt(hi, pre[:, n % 2, :], small[:, 3, 0:1].to_broadcast([P, T]), ALU.mult).then_inc(s_hhi, 1)
                            pool.wait_ge(s_hhi, count(bb, 8, i))
                            tt(lo, pre[:, n % 2, :], hi.bitcast(F32), ALU.subtract).then_inc(s_hlo, 1)

            pool.wait_ge(s_const, 16 * NCONST)
            runs(pool, body)


def kernel(**inputs):
    import concourse.bacc as bacc
    from concourse.bass_utils import run_bass_kernel_spmd

    a = {n.removeprefix("L0_"): np.asarray(v) for n, v in inputs.items()}
    wq, wk, wv = (a[f"attn_W{n}"].reshape(D, H, DK) for n in "qkv")
    arrays = {
        "x": a["attn_x"],
        "w_left": np.stack([wq, wk], 2).reshape(D, 8 * P),
        "w_kv": np.stack([wk.reshape(D, NG, P), wv.reshape(D, NG, P)], 2).reshape(D, 2 * 512),
        "w_o": a["attn_Wo"],
        "w_1": a["ffn_w1_w"].T, "w_2": a["ffn_w2_w"].T,
        "h_1": a["ffn_h1_w"].T.reshape(NM, P, HID).transpose(1, 0, 2).reshape(P, NM * HID),
        "h_2": a["ffn_h2_w"].T.reshape(NM, P, HID).transpose(1, 0, 2).reshape(P, NM * HID),
        "w_3": a["ffn_w3_w"].T,
        "f_1": a["ffn_w1_s"].reshape(NM, P).T, "f_2": a["ffn_w2_s"].reshape(NM, P).T,
        "f_h1": a["ffn_h1_s"].reshape(NM, P).T, "f_h2": a["ffn_h2_s"].reshape(NM, P).T,
        "f_3": np.broadcast_to(a["ffn_w3_s"][None, :], (P, D)),
    }
    arrays = {n: np.ascontiguousarray(v) for n, v in arrays.items()}
    names = list(arrays)
    arrays |= constants()

    nc = bacc.Bacc("TRN2", target_bir_lowering=False, num_devices=1)
    aps = {n: nc.dram_tensor(n, v.shape, F32, kind="ExternalInput").ap() for n, v in arrays.items()}
    out = nc.dram_tensor("out", (B, T, D), F32, kind="ExternalOutput").ap()
    build(nc, *[aps[n] for n in names], {n: v for n, v in aps.items() if n.startswith("c_")}, out)
    r = run_bass_kernel_spmd(nc, [arrays], core_ids=[0])
    return r.results[0]["out"]
```

```python
from contextlib import ExitStack

import numpy as np

import concourse.bass as bass
from concourse import mybir

B, T, D = 16, 512, 128
H, DK = 16, 32
HID = 512
DECAY = 0.99
EPS = 1e-5
P = 128
NG = H // 4
NC = T // P
ITEMS = NG * NC
NU = NG * (NC - 1)
NM = HID // P

F32 = mybir.dt.float32
F32R = mybir.dt.float32r
ALU = mybir.AluOpType
ACT = mybir.ActivationFunctionType

NEWTON = 1
ROOT_STEPS = 2 + 5 * NEWTON

LOAD, LN1, XT, PROJ = -16, -15, -9, -8
LOAD_RES, WO, LN2A, LN2B, XT2, KEEP, W12, H1, H2, W3, LN3 = 8, 18, 20, 21, 22, 23, 23, 27, 31, 36, 39
FIRST_LOOPED, END_LOOPED = 3, B - 1
FIRST, END = -1, B + 2


def fills(slot):
    steps = []
    for g in range(NG):
        steps += [(use, n, PROJ + 4 * g + i) for i, (use, n) in
                  enumerate([("left", 2 * g), ("left", 2 * g + 1), ("kv", 2 * g), ("kv", 2 * g + 1)])]
    steps += [("wo", n, WO + n) for n in range(2)]
    steps += [(kind, m, W12 + m) for m in range(NM) for kind in ("gate", "up")]
    steps += [(kind, m, off + m) for kind, off in (("h1", H1), ("h2", H2)) for m in range(NM)]
    steps += [("w3", n, W3 + n) for n in range(2)]
    steps += [("xt2", 0, XT2), ("xt", 0, XT)]
    steps = [s for s in steps if s[2] % ITEMS == slot]
    if slot % 2 == 0 and len(steps) == 2 and steps[1][0] in ("h1", "h2", "w3"):
        steps.reverse()
    return steps


def mid_fills(slot):
    return fills(slot)[:(len(fills(slot)) + 1) // 2]


def end_fills(slot):
    return fills(slot)[(len(fills(slot)) + 1) // 2:]


RING = [(s, *use) for s in range(ITEMS) for use in fills(s)]
assert len(RING) % 2 == 0


def constants():
    k = DECAY ** -np.arange(T, dtype=np.float64)
    r, t = np.arange(P)[:, None], np.arange(P)[None, :]
    tri = (r <= t).astype(np.float64)
    p_mask = np.stack([tri / k[c * P:(c + 1) * P][None, :] for c in range(NC)], 1)
    d_mask = tri * (DECAY ** (t - r).astype(np.float64) - 1.0)
    quad = np.arange(P) // DK
    right_scale = np.where((quad % 2 == 1)[:, None], k[None, :], 1.0)
    tok_kappa = k.reshape(NC, P).T
    eps_t = EPS * k.reshape(NC, P).T ** 4
    sk = np.zeros((P, 2, 2, DK))
    e = np.zeros((P, 2, DK))
    for row in range(P):
        h, part = quad[row] // 2, quad[row] % 2
        sk[row, h] = 1.0 if part == 0 else 0.0
        if part:
            sk[row, h, 0] = -1.0
        e[row, h] = 1.0
    out = {"c_tri": tri, "c_pmask": p_mask.reshape(P, NC * P), "c_dmask": d_mask,
           "c_rscale": right_scale, "c_kappa": tok_kappa, "c_eps": eps_t,
           "c_kappa1": np.stack([tok_kappa, np.ones((P, NC))], 2).reshape(P, -1),
           "c_small": np.tile(np.repeat([-0.5, 1.5, EPS, 1.0], NC), (P, 1)),
           "c_sk": sk.reshape(P, -1), "c_e": e.reshape(P, -1), "c_id": np.eye(P)}
    return {n: np.ascontiguousarray(a.astype(np.float32)) for n, a in out.items()}


def build(nc, x, w_left, w_kv, w_o, w_1, w_2, h_1, h_2, w_3, f_1, f_2, f_h1, f_h2, f_3, tables, out):
    with ExitStack() as ctx:
        def sb(name, shape, dt=F32):
            return ctx.enter_context(nc.sbuf_tensor(name, shape, dt))

        def bank(name):
            return ctx.enter_context(nc.psum_tensor(name, [P, 512], F32))

        def sem(name):
            return ctx.enter_context(nc.semaphore(name))

        def halves(name, n):
            return sb(name + "_hi", [P, n], F32R), sb(name + "_lo", [P, n], F32R)
        wl, wkv = halves("wl", 8 * P), halves("wkv", 2 * 512)
        w1, w2 = halves("w1", HID), halves("w2", HID)
        wh1, wh2 = halves("wh1", NM * HID), halves("wh2", NM * HID)
        wo = sb("wo", [P, NG, D])
        w3 = sb("w3", [P, NM, D])
        sc1, sc2, sch1, sch2 = (sb(n, [P, NM]) for n in ("sc1", "sc2", "sch1", "sch2"))

        tri, dmask = sb("tri", [P, P]), sb("dmask", [P, P])
        pmask = sb("pmask", [P, NC, P])
        rscale = sb("rscale", [P, T])
        kappa, eps_t = sb("kappa", [P, NC]), sb("eps_t", [P, NC])
        kappa1 = sb("kappa1", [P, NC, 2])
        skmask = sb("skmask", [P, 2, 2 * DK])
        emask = sb("emask", [P, 2, DK])
        ident = sb("ident", [P, P])
        low_top, flag = sb("low_top", [P, 4]), sb("flag", [1, 1])
        small, held = sb("small", [P, 4, NC]), sb("held", [P, 1])

        xin, x2, x2_kept = sb("xin", [P, NC, D]), sb("x2", [P, NC, D]), sb("x2_kept", [P, NC, D])
        xn2 = sb("xn2", [P, NC, D])
        stats, mv = sb("stats", [P, 4, NC, 6]), sb("mv", [P, 4, NC, 2])
        rstd, newton = sb("rstd", [P, 4, NC]), sb("newton", [P, 4, NC])
        xt, xt2 = halves("xt", T), halves("xt2", T)
        left, right = sb("left", [P, NG, 2, T]), sb("right", [P, NG, 2, T])
        kn, vn = sb("kn", [P, NG, NC, P]), sb("vn", [P, NG, NC, P])
        kk = sb("kk", [P, 2, 4, 2, DK])
        pm, dm, wt = sb("pm", [P, 2, 4, P]), sb("dm", [P, 2, 4, P]), sb("wt", [P, 2, 4, P])
        skbd = sb("skbd", [P, 2, 2, 2 * DK])
        ebd = sb("ebd", [P, 2, 2, DK])
        qpn = sb("qpn", [P, 2, 2, P])
        ot = sb("ot", [P, NG, T])
        silu = sb("silu", [P, HID])
        pre = sb("pre", [P, 2, T])
        hid, gel = halves("hid", NM * T), halves("gel", NM * T)
        gel2 = sb("gel2", [P, NM, T])
        outt = gel2[:, 0, :].rearrange("p (c d) -> p c d", c=NC)

        ps_aw = ctx.enter_context(nc.psum_tensor("ps_aw", [P, 2, 512], F32))
        ps_x, ps_o = bank("ps_x"), bank("ps_o")
        ps_sk, ps_e = bank("ps_sk"), bank("ps_e")
        ps_f = [bank("ps_f0"), bank("ps_f1")]
        aw_v = ps_aw[:].rearrange("p k (w r t) -> p w r k t", w=2, r=2)
        a_v, w_v = aw_v[:, 0], aw_v[:, 1]
        x_v = ps_x[:, 0:2 * P].rearrange("p (r t) -> p r t", r=2)
        t_v = ps_o[:, P:3 * P].rearrange("p (r t) -> p r t", r=2)
        sk_v = ps_sk[:, 0:4 * DK].rearrange("p (r f) -> p r f", r=2)
        e_v = ps_e[:, 0:2 * DK].rearrange("p (r f) -> p r f", r=2)
        f_v = [b[:].rearrange("p (c d) -> p c d", c=4) for b in ps_f]

        s_first, s_const, s_hi, s_split, s_w3s = sem("first_const_loaded"), sem("const_loaded"), sem("weights_hi"), sem("weights_split"), sem("w3_scaled")
        s_x, s_xr, s_out = sem("x_loaded"), sem("xres_loaded"), sem("out_stored")
        s_ln = [sem(f"ln{i}_step") for i in range(4)]
        s_xt, s_xhi, s_xlo = sem("xt_ready"), sem("xt_hi"), sem("xt_lo")
        s_xt2, s_x2hi, s_x2lo = sem("xt2_ready"), sem("xt2_hi"), sem("xt2_lo")
        s_left, s_kv = sem("left_ready"), sem("kv_ready")
        s_leftc, s_rightc, s_kn, s_vn = sem("left_copied"), sem("right_copied"), sem("k_copied"), sem("v_copied")
        s_kk = sem("kappa_k")
        s_a, s_m = sem("scores_ready"), sem("scores_masked")
        s_xr_, s_p, s_d = sem("pd_ready"), sem("p_copied"), sem("d_copied")
        s_sk, s_skbd = sem("sk_ready"), sem("sk_spread")
        s_t, s_qpn = sem("qp_turned"), sem("qp_copied")
        s_w, s_wt = sem("weights_ready"), sem("weights_masked")
        s_o, s_ot = sem("o_ready"), sem("o_copied")
        s_e, s_ebd = sem("e_ready"), sem("e_spread")
        s_y, s_x2 = sem("y_ready"), sem("x2_added")
        s_gate, s_up, s_silu, s_h = sem("gate_ready"), sem("up_ready"), sem("silu_done"), sem("h_done")
        s_hhi, s_hlo = sem("pre_hi"), sem("pre_lo")
        s_h1, s_g1, s_h2, s_g2 = sem("h1_ready"), sem("gelu1_done"), sem("h2_ready"), sem("gelu2_done")
        s_w3, s_fin = sem("w3_ready"), sem("out_added")
        s_q = sem("q_copied")
        s_low, s_flag = sem("low_halves_reduced"), sem("flag_ready")
        s_res = sem("x2_kept")
        s_yc, s_w3c = sem("y_copied"), sem("w3_copied")
        s_root = [sem(f"ln{i}_root_step") for i in range(4)]

        def count(bb, per, index):
            return bb * per + (index + 1)

        def due(n):
            return not isinstance(n, int) or n > 0

        def has(it, off):
            return not isinstance(it, int) or 0 <= it - off // ITEMS < B

        def batch(it, off):
            return it - off // ITEMS

        def items(it, slot, lag):
            j = slot - lag
            bb = it if j >= 0 else it - 1
            if isinstance(bb, int) and not 0 <= bb < B:
                return None
            j %= ITEMS
            return bb, j, j // NC, j % NC

        def runs(eng, body, first=FIRST):
            for it in range(first, FIRST_LOOPED):
                body(it)
            with eng.Fori(FIRST_LOOPED, END_LOOPED) as it:
                body(it)
            for it in range(END_LOOPED, END):
                body(it)

        def freed_by(kind, n):
            return {
                "xt": [(s_xhi, 1, 0), (s_xlo, 1, 0)],
                "xt2": [(s_x2hi, 1, 0), (s_x2lo, 1, 0)],
                "left": [(s_leftc, 8, n)],
                "kv": [(s_kn, 8, n), (s_vn, 8, n)],
                "wo": [(s_yc, 2, n)], "w3": [(s_w3c, 2, n)],
                "gate": [(s_silu, 4, n)], "up": [(s_h, 4, n)],
                "h1": [(s_g1, 4, n)], "h2": [(s_g2, 4, n)],
            }[kind]

        def ring_place(kind, n):
            return next(i for i, u in enumerate(RING) if u[1:3] == (kind, n))

        def fill_bank(kind, n):
            return ring_place(kind, n) % 2

        def wait_bank_free(pe, it, kind, n):
            i = ring_place(kind, n)
            for back in range(2, 3 * len(RING), 2):
                turn, at = divmod(i - back, len(RING))
                _, pkind, pn, poff = RING[at]
                pit = it + turn
                if isinstance(pit, int) and not 0 <= pit - poff // ITEMS < B:
                    if pit < FIRST:
                        return
                    continue
                for s, per, index in freed_by(pkind, pn):
                    pe.wait_ge(s, count(batch(pit, poff), per, index))
                return

        NCONST = 9 + 4 + 3
        block = ctx.enter_context(nc.Block())

        def flat(tile):
            return tile.rearrange("p a b -> p (a b)")
        ffn_stage = [gel2[:, i, :] for i in range(NM)] + [ot[:, i, :] for i in range(NG)] + [pre[:, i, :] for i in range(2)]
        parts = [(w_1, w1), (w_2, w2)] + [(src[:, k * HID:(k + 1) * HID], [x_[:, k * HID:(k + 1) * HID] for x_ in pair])
                                          for src, pair in ((h_1, wh1), (h_2, wh2)) for k in range(NM)]
        raw = [(w_left, flat(left[:, 2]), wl), (w_kv, flat(left[:, 3]), wkv)] + [
            (src, stage, pair) for (src, pair), stage in zip(parts, ffn_stage)]
        raw3 = right[:, 3, 0, :].rearrange("p (m d) -> p m d", m=NM)
        row3 = right[:, 3, 1, 0:D]
        NRAW = len(raw)
        s_raw = [sem(f"raw_weights{n}_loaded") for n in range(NRAW)]

        @block.sync
        def _(sp):
            consts = [(tri[:], "c_tri"), (dmask[:], "c_dmask"), (pmask[:].rearrange("p c t -> p (c t)"), "c_pmask"),
                      (rscale[:], "c_rscale"), (kappa[:], "c_kappa"), (eps_t[:], "c_eps"),
                      (skmask[:].rearrange("p a b -> p (a b)"), "c_sk"), (emask[:].rearrange("p a b -> p (a b)"), "c_e"),
                      (kappa1[:].rearrange("p a b -> p (a b)"), "c_kappa1")]

            def load(it):
                if has(it, LOAD):
                    bb = batch(it, LOAD)
                    if due(seen := count(bb, 1, -1)):
                        sp.wait_ge(s_xt, seen)
                    sp.dma_start(xin[:], x[bb].rearrange("(c p) d -> p c d", p=P)).then_inc(s_x, 16)

            def body(it):
                for slot in range(ITEMS):
                    if slot == LOAD % ITEMS and it is not FIRST:
                        load(it)
                    if slot == LOAD_RES % ITEMS and has(it, LOAD_RES):
                        bb = batch(it, LOAD_RES)
                        if due(seen := count(bb, 1, -1)):
                            sp.wait_ge(s_xt2, seen)
                        sp.dma_start(xn2[:], x[bb].rearrange("(c p) d -> p c d", p=P)).then_inc(s_xr, 16)
                    if slot == LN3 % ITEMS and has(it, LN3):
                        bb = batch(it, LN3)
                        sp.wait_ge(s_fin, count(bb, 1, 0))
                        sp.dma_start(out[bb].rearrange("(c p) d -> p c d", p=P), outt).then_inc(s_out, 16)
            load(FIRST)
            for dst, name in ((small[:].rearrange("p a b -> p (a b)"), "c_small"), (ident[:], "c_id")):
                sp.dma_start(dst, tables[name]).then_inc(s_first, 16)
            for n, (src, stage, _) in enumerate(raw[:2]):
                sp.dma_start(stage, src).then_inc(s_raw[n], 16)
            for n, (dst, name) in enumerate(consts):
                sp.dma_start(dst, tables[name]).then_inc(s_const, 16)
            for dst, src in ((sc1, f_1), (sc2, f_2), (sch1, f_h1), (sch2, f_h2)):
                sp.dma_start(dst[:], src).then_inc(s_const, 16)
            sp.dma_start(wo[:], w_o.rearrange("(g p) d -> p g d", p=P)).then_inc(s_const, 16)
            sp.dma_start(raw3, w_3.rearrange("(m p) d -> p m d", p=P)).then_inc(s_const, 16)
            sp.dma_start(row3, f_3).then_inc(s_const, 16)
            for n, (src, stage, _) in enumerate(raw[2:], 2):
                sp.dma_start(stage, src).then_inc(s_raw[n], 16)
            runs(sp, body)
            sp.wait_ge(s_out, 16 * B)
        @block.tensor
        def _(pe):
            mm = nc.tensor.matmul

            def three(dst, lo_hi_l, lo_hi_r, start=True, stop=True, low_zero=False):
                (lh, ll), (rh, rl) = lo_hi_l, lo_hi_r
                if not low_zero:
                    mm(dst, ll, rh, start=start, stop=False)
                mm(dst, lh, rl, start=start and low_zero, stop=False)
                return mm(dst, lh, rh, start=False, stop=stop)

            def scores(bb, j, g, c):
                n = count(bb, ITEMS, j)
                if c == 0:
                    pe.wait_ge(s_leftc, count(bb, 8, 2 * g + 1))
                    pe.wait_ge(s_rightc, count(bb, 8, 2 * g + 1))
                if due(seen := n - 1):
                    pe.wait_ge(s_m, seen)
                if due(seen := n - 3):
                    pe.wait_ge(s_wt, seen)
                for h in range(4):
                    r, q = h // 2, 64 * (h % 2) + DK
                    m = mm(a_v[:, r, h % 2, :], left[q:q + DK, g, r, c * P:(c + 1) * P],
                           right[q:q + DK, g, r, c * P:(c + 1) * P], start=True, stop=True)
                m.then_inc(s_a, 1)

            def pd(bb, j, g, c):
                n, b2 = count(bb, ITEMS, j), j % 2
                if c == 0:
                    pe.wait_ge(s_kn, count(bb, 8, 2 * g + 1))
                else:
                    if due(seen := count(bb, NU, 3 * g + c - 1)):
                        pe.wait_ge(s_skbd, seen)
                pe.wait_ge(s_m, n)
                if due(seen := n - 1):
                    pe.wait_ge(s_p, seen)
                if due(seen := n - 1):
                    pe.wait_ge(s_d, seen)
                for r in range(2):
                    if c:
                        mm(x_v[:, r, :], skbd[:, r].rearrange("p a b -> p (a b)"), right[:, g, r, c * P:(c + 1) * P],
                           start=True, stop=False, skip_group_check=True)
                    for part, src in ((0, dm), (1, pm)):
                        for hh in range(2):
                            q, h = 64 * hh + DK * part, 2 * r + hh
                            m = mm(x_v[q:q + DK, r, :], kn[:, g, c, h * DK:(h + 1) * DK], src[:, b2, h, :],
                                   start=(c == 0), stop=True, skip_group_check=True)
                m.then_inc(s_xr_, 1)

            def update_sk(bb, j, g, c):
                u = 3 * g + c
                pe.wait_ge(s_kk, count(bb, NU, u))
                if due(seen := count(bb, NU, u - 1)):
                    pe.wait_ge(s_skbd, seen)
                for r in range(2):
                    for hh in range(2):
                        h, q = 2 * r + hh, 64 * hh
                        kh = kn[:, g, c, h * DK:(h + 1) * DK]
                        mm(sk_v[q:q + DK, r, :], kh, kk[:, u % 2, h].rearrange("p a b -> p (a b)"),
                           start=(c == 0 and r == 0), stop=True, skip_group_check=True)
                        m = mm(sk_v[q + DK:q + 2 * DK, r, 0:DK], kh, kh, start=(c == 0 and r == 0), stop=True,
                               skip_group_check=True)
                m.then_inc(s_sk, 1)

            def turn_qp(bb, j, g, c):
                u = 3 * g + c
                pe.wait_ge(s_p, count(bb, ITEMS, j))
                if due(seen := count(bb, NU, u - 1)):
                    pe.wait_ge(s_qpn, seen)
                if due(seen := count(bb, ITEMS, j) - 2):
                    pe.wait_ge(s_ot, seen)
                for r in range(2):
                    m = nc.tensor.transpose(t_v[:, r, :], left[:, g, r, c * P:(c + 1) * P], ident[:])
                m.then_inc(s_t, 1)

            def weights(bb, j, g, c, newest):
                n = count(bb, ITEMS, j)
                if newest:
                    pe.wait_ge(s_m, count(newest[0], ITEMS, newest[1]))
                pe.wait_ge(s_p, n)
                pe.wait_ge(s_d, n)
                if due(seen := n - 1):
                    pe.wait_ge(s_wt, seen)
                for h in range(4):
                    r, q = h // 2, 64 * (h % 2)
                    m = mm(w_v[:, r, h % 2, :], left[q:q + 64, g, r, c * P:(c + 1) * P],
                           right[q:q + 64, g, r, c * P:(c + 1) * P], start=True, stop=True)
                m.then_inc(s_w, 1)

            def outputs(bb, j, g, c):
                n, b2 = count(bb, ITEMS, j), j % 2
                if c == 0:
                    pe.wait_ge(s_vn, count(bb, 8, 2 * g + 1))
                else:
                    if due(seen := count(bb, NU, 3 * g + c - 1)):
                        pe.wait_ge(s_ebd, seen)
                pe.wait_ge(s_wt, n)
                if due(seen := n - 1):
                    pe.wait_ge(s_ot, seen)
                if c:
                    for r in range(2):
                        mm(ps_o[64 * r:64 * r + 64, 0:P], ebd[:, r].rearrange("p a b -> p (a b)"),
                           right[:, g, r, c * P:(c + 1) * P], start=True, stop=False, skip_group_check=True)
                for h in range(4):
                    m = mm(ps_o[DK * h:DK * h + DK, 0:P], vn[:, g, c, h * DK:(h + 1) * DK], wt[:, b2, h, :],
                           start=(c == 0), stop=True, skip_group_check=True)
                m.then_inc(s_o, 1)

            def update_e(bb, j, g, c):
                u = 3 * g + c
                pe.wait_ge(s_qpn, count(bb, NU, u))
                if due(seen := count(bb, NU, u - 1)):
                    pe.wait_ge(s_ebd, seen)
                for r in range(2):
                    for hh in range(2):
                        h = 2 * r + hh
                        m = mm(e_v[64 * hh:64 * hh + 64, r, :], qpn[:, u % 2, r, 64 * hh:64 * hh + 64],
                               vn[:, g, c, h * DK:(h + 1) * DK], start=(c == 0 and r == 0), stop=True,
                               skip_group_check=True)
                m.then_inc(s_e, 1)

            def cols(pair, a, b):
                return pair[0][:, a:b], pair[1][:, a:b]

            def fill(it, kind, n, off, low_zero):
                bb = batch(it, off)
                wait_bank_free(pe, it, kind, n)
                f = fill_bank(kind, n)
                dst = ps_f[f]
                if kind in ("xt", "xt2"):
                    src, s, t = (xin, s_ln[0], s_xt) if kind == "xt" else (xn2, s_ln[2], s_xt2)
                    pe.wait_ge(s, count(bb, 3, 2))
                    for c in range(NC):
                        m = nc.tensor.transpose(f_v[f][:, c, :], src[:, c, :], ident[:])
                    m.then_inc(t, 1)
                elif kind == "left":
                    if isinstance(bb, int) and bb == 0 and n == 0:
                        pe.wait_ge(s_split, 2)
                    pe.wait_ge(s_xlo, count(bb, 1, 0))
                    three(dst[:], cols(wl, n * P, (n + 1) * P), (xt[0][:], xt[1][:])).then_inc(s_left, 1)
                elif kind == "kv":
                    pe.wait_ge(s_xlo, count(bb, 1, 0))
                    g = n // 2
                    for i in range(2):
                        c = 2 * (n % 2) + i
                        m = three(dst[:, 256 * i:256 * i + 256], cols(xt, c * P, (c + 1) * P), cols(wkv, 256 * g, 256 * g + 256))
                    m.then_inc(s_kv, 1)
                elif kind == "wo":
                    if due(seen := count(bb, ITEMS, ITEMS - NC + 2 * n + 1)):
                        pe.wait_ge(s_ot, seen)
                    for c in (2 * n, 2 * n + 1):
                        for g in range(NG):
                            m = mm(f_v[f][:, c, :], ot[:, g, c * P:(c + 1) * P], wo[:, g, :], start=(g == 0), stop=(g == NG - 1))
                    m.then_inc(s_y, 1)
                elif kind in ("gate", "up"):
                    pe.wait_ge(s_x2lo, count(bb, 1, 0))
                    w, s = (w1, s_gate) if kind == "gate" else (w2, s_up)
                    if isinstance(bb, int) and bb == 0 and n == 0:
                        pe.wait_ge(s_split, NRAW)
                        pe.wait_ge(s_w3s, 1)
                    three(dst[:], cols(w, n * P, (n + 1) * P), (xt2[0][:], xt2[1][:]), low_zero=low_zero).then_inc(s, 1)
                elif kind in ("h1", "h2"):
                    w, src, s = (wh1, hid, s_h1) if kind == "h1" else (wh2, gel, s_h2)
                    for k in range(NM):
                        if n == 0:
                            pe.wait_ge(s_hlo, count(bb, 8, k + (4 if kind == "h2" else 0)))
                        m = three(dst[:], cols(w, k * HID + n * P, k * HID + (n + 1) * P), cols(src, k * T, (k + 1) * T),
                                  start=(k == 0), stop=(k == NM - 1), low_zero=low_zero)
                    m.then_inc(s, 1)
                elif kind == "w3":
                    pe.wait_ge(s_g2, count(bb, 4, 3))
                    for c in (2 * n, 2 * n + 1):
                        for k in range(NM):
                            m = mm(f_v[f][:, c, :], gel2[:, k, c * P:(c + 1) * P], w3[:, k, :], start=(k == 0), stop=(k == NM - 1))
                    m.then_inc(s_w3, 1)

            def body(it, low_zero=False):
                for slot in range(ITEMS):
                    i0, i1, i2, i3 = (items(it, slot, lag) for lag in range(4))
                    if i0:
                        scores(*i0)
                    if i1:
                        pd(*i1)
                        if i1[3] < NC - 1:
                            update_sk(*i1)
                    if i2 and i2[3] < NC - 1:
                        turn_qp(*i2)
                    for kind, n, off in mid_fills(slot):
                        if has(it, off):
                            fill(it, kind, n, off, low_zero)
                    if i2:
                        weights(*i2, i0)
                    if i3:
                        if i2 and i2[3] < NC - 1:
                            pe.wait_ge(s_qpn, count(i2[0], NU, 3 * i2[2] + i2[3]))
                        outputs(*i3)
                        if i3[3] < NC - 1:
                            update_e(*i3)
                    for kind, n, off in end_fills(slot):
                        if has(it, off):
                            fill(it, kind, n, off, low_zero)

            pe.wait_ge(s_first, 16 * 2)
            body(FIRST)
            pe.wait_ge(s_const, 16 * NCONST)
            body(FIRST + 1)
            pe.wait_ge(s_flag, 1)
            low_max = pe.value_load(flag[0:1, 0:1].bitcast(mybir.dt.int32))
            with pe.If(low_max == 0):
                runs(pe, lambda it: body(it, True), FIRST + 2)
            with pe.Else():
                runs(pe, body, FIRST + 2)


        @block.scalar
        def _(act):
            fn = nc.scalar.activation

            def body(it):
                for slot in range(ITEMS):
                    if isinstance(it, int) and it == FIRST and slot == PROJ % ITEMS:
                        act.wait_ge(s_const, 16 * NCONST)
                    i1, i2, i3 = (items(it, slot, lag) for lag in (1, 2, 3))
                    if i1:
                        bb, j, g, c = i1
                        act.wait_ge(s_xr_, count(bb, ITEMS, j))
                        for hh in range(2):
                            q = 64 * hh + DK
                            m = fn(left[q:q + DK, g, :, c * P:(c + 1) * P], x_v[q:q + DK, :, :], ACT.Copy)
                        m.then_inc(s_p, 1)
                        for hh in range(2):
                            q = 64 * hh
                            m = fn(right[q:q + DK, g, :, c * P:(c + 1) * P], x_v[q:q + DK, :, :], ACT.Copy)
                        m.then_inc(s_d, 1)
                    if i2 and i2[3] < NC - 1:
                        bb, j, g, c = i2
                        u = 3 * g + c
                        act.wait_ge(s_t, count(bb, NU, u))
                        if due(seen := count(bb, NU, u - 2)):
                            act.wait_ge(s_e, seen)
                        fn(qpn[:, u % 2], t_v[:, :, :], ACT.Copy).then_inc(s_qpn, 1)
                    for kind, n, off in mid_fills(slot):
                        if has(it, off):
                            fill(it, kind, n, off)
                    if i3:
                        bb, j, g, c = i3
                        act.wait_ge(s_o, count(bb, ITEMS, j))
                        if g == 0:
                            if due(seen := count(bb, 2, c // 2 - 2)):
                                act.wait_ge(s_y, seen)
                        fn(ot[:, g, c * P:(c + 1) * P], ps_o[:, 0:P], ACT.Copy).then_inc(s_ot, 1)
                    for kind, n, off in end_fills(slot):
                        if has(it, off):
                            fill(it, kind, n, off)
                    if isinstance(it, int) and it == FIRST and 6 <= slot < 6 + NRAW - 2:
                        high_half(slot - 4)

            def fill(it, kind, n, off):
                bb = batch(it, off)
                f = fill_bank(kind, n)
                src = ps_f[f][:]
                if kind == "xt":
                    act.wait_ge(s_xt, count(bb, 1, 0))
                    if due(seen := count(bb, 8, -1)):
                        act.wait_ge(s_kv, seen)
                    if due(seen := count(bb, 1, -1)):
                        act.wait_ge(s_xlo, seen)
                    fn(xt[0][:], src, ACT.Copy).then_inc(s_xhi, 1)
                elif kind == "xt2":
                    act.wait_ge(s_xt2, count(bb, 1, 0))
                    if due(seen := count(bb, 4, -1)):
                        act.wait_ge(s_up, seen)
                    if due(seen := count(bb, 1, -1)):
                        act.wait_ge(s_x2lo, seen)
                    fn(xt2[0][:], src, ACT.Copy).then_inc(s_x2hi, 1)
                elif kind == "left":
                    g = n // 2
                    act.wait_ge(s_left, count(bb, 8, n))
                    if due(seen := count(bb, ITEMS, 4 * g + 3 - ITEMS)):
                        act.wait_ge(s_w, seen)
                    fn(left[:, g, n % 2, :], src, ACT.Copy)
                    if due(seen := count(bb, ITEMS, 4 * g + 3 - ITEMS)):
                        act.wait_ge(s_o, seen)
                    fn(right[:, g, n % 2, :], src, ACT.Copy).then_inc(s_q, 1)
                    act.wait_ge(s_q, count(bb, 8, n))
                    for hh in range(2):
                        q = 64 * hh
                        m = fn(right[q + DK:q + 2 * DK, g, n % 2, :], ps_f[f][q:q + DK, :], ACT.Copy)
                    m.then_inc(s_leftc, 1)
                elif kind == "wo":
                    act.wait_ge(s_y, count(bb, 2, n))
                    if due(seen := count(bb, 1, -1)):
                        act.wait_ge(s_res, seen)
                    fn(x2[:, 2 * n:2 * n + 2, :], f_v[f][:, 2 * n:2 * n + 2, :], ACT.Copy).then_inc(s_yc, 1)
                elif kind == "w3":
                    act.wait_ge(s_w3, count(bb, 2, n))
                    fn(outt[:, 2 * n:2 * n + 2, :], f_v[f][:, 2 * n:2 * n + 2, :], ACT.Copy).then_inc(s_w3c, 1)
                elif kind == "kv":
                    g = n // 2
                    act.wait_ge(s_kv, count(bb, 8, n))
                    if due(seen := count(bb, ITEMS, 4 * g + 3 - ITEMS)):
                        act.wait_ge(s_xr_, seen)
                    v = src.rearrange("p (i k d) -> p i k d", i=2, k=2)
                    c = 2 * (n % 2)
                    fn(kn[:, g, c:c + 2, :], v[:, :, 0, :], ACT.Copy).then_inc(s_kn, 1)
                elif kind == "gate":
                    act.wait_ge(s_gate, count(bb, 4, n))
                    if due(seen := count(bb, 4, n - 1)):
                        act.wait_ge(s_h, seen)
                    fn(silu[:], src, ACT.Silu, scale=sc1[:, n:n + 1]).then_inc(s_silu, 1)
                elif kind == "h1":
                    act.wait_ge(s_h1, count(bb, 4, n))
                    if due(seen := count(bb, 8, 4 + n - 2)):
                        act.wait_ge(s_hlo, seen)
                    fn(pre[:, n % 2, :], src, ACT.Gelu, scale=sch1[:, n:n + 1]).then_inc(s_g1, 1)
                elif kind == "h2":
                    act.wait_ge(s_h2, count(bb, 4, n))
                    if due(seen := 16 * count(bb, 1, -1)):
                        act.wait_ge(s_out, seen)
                    fn(gel2[:, n, :], src, ACT.Gelu, scale=sch2[:, n:n + 1]).then_inc(s_g2, 1)

            def high_half(n):
                _, stage, (hi, _) = raw[n]
                act.wait_ge(s_raw[n], 16)
                fn(hi[:], stage, ACT.Copy).then_inc(s_hi, 1)

            for n in range(2):
                high_half(n)
            runs(act, body)

        @block.vector
        def _(dve):
            tt, ts = nc.vector.tensor_tensor, nc.vector.tensor_scalar

            def per_head(m):
                return m.unsqueeze(1).unsqueeze(1).to_broadcast([P, 2, 2, P])

            def pairs(tile):
                return tile.rearrange("p (r k) t -> p r k t", r=2)

            LNS = (("ln1", LN1, s_x, 16, xin, xin), ("ln2a", LN2A, s_yc, 2, x2, x2), ("ln2b", LN2B, s_x2, 1, x2, xn2),
                   ("ln3", LN3, s_w3c, 2, outt, outt))

            def moments(which, bb):
                s, (_, _, made, step, src, _) = s_ln[which], LNS[which]
                dve.wait_ge(made, step * count(bb, 1, 0))
                for c in range(NC):
                    m = nc.vector.bn_stats(stats[:, which, c, :], src[:, c, :])
                m.then_inc(s, 1)
                dve.wait_ge(s, count(bb, 3, 0))
                nc.vector.tensor_copy(held[:], small[:, 0, 0:1])
                for c in range(NC):
                    m = nc.vector.bn_aggr(mv[:, which, c, :], stats[:, which, c, :])
                m.then_inc(s, 1)

            def normalise(which, bb):
                s, (_, _, _, _, src, dst) = s_ln[which], LNS[which]
                dve.wait_ge(s_root[which], count(bb, ROOT_STEPS, ROOT_STEPS - 1))
                for c in range(NC):
                    m = ts(dst[:, c, :], src[:, c, :], mv[:, which, c, 0:1], rstd[:, which, c:c + 1], ALU.subtract, ALU.mult)
                m.then_inc(s, 1)

            def body(it):
                for slot in range(ITEMS):
                    if isinstance(it, int) and it == FIRST and slot == PROJ % ITEMS:
                        dve.wait_ge(s_const, 16 * NCONST)
                        tt(w3[:], raw3, row3.unsqueeze(1).to_broadcast([P, NM, D]), ALU.mult).then_inc(s_w3s, 1)
                    i0, i1, i2, i3 = (items(it, slot, lag) for lag in range(4))
                    if i0:
                        bb, j, g, c = i0
                        n = count(bb, ITEMS, j)
                        dve.wait_ge(s_a, n)
                        if due(seen := n - 2):
                            dve.wait_ge(s_xr_, seen)
                        tt(pairs(pm[:, j % 2]), a_v, per_head(pmask[:, c, :]), ALU.mult)
                        tt(pairs(dm[:, j % 2]), a_v, per_head(dmask[:]), ALU.mult).then_inc(s_m, 1)
                    if i1:
                        bb, j, g, c = i1
                        if c < NC - 1:
                            dve.wait_ge(s_sk, count(bb, NU, 3 * g + c))
                            tt(skbd[:], sk_v.unsqueeze(2).to_broadcast([P, 2, 2, 2 * DK]),
                               skmask[:].unsqueeze(1).to_broadcast([P, 2, 2, 2 * DK]), ALU.mult).then_inc(s_skbd, 1)
                    for which, (_, off, *_) in enumerate(LNS):
                        if slot == off % ITEMS and has(it, off):
                            moments(which, batch(it, off))
                    for kind, n, off in mid_fills(slot):
                        if has(it, off):
                            fill(it, kind, n, off)
                    if i2:
                        bb, j, g, c = i2
                        n = count(bb, ITEMS, j)
                        dve.wait_ge(s_w, n)
                        if due(seen := n - 2):
                            dve.wait_ge(s_o, seen)
                        tt(pairs(wt[:, j % 2]), w_v, per_head(tri[:]), ALU.mult).then_inc(s_wt, 1)
                    if i3 and i3[3] < NC - 1:
                        bb, j, g, c = i3
                        dve.wait_ge(s_e, count(bb, NU, 3 * g + c))
                        tt(ebd[:], e_v.unsqueeze(2).to_broadcast([P, 2, 2, DK]), emask[:].unsqueeze(1).to_broadcast([P, 2, 2, DK]),
                           ALU.mult).then_inc(s_ebd, 1)
                    for kind, n, off in end_fills(slot):
                        if has(it, off):
                            fill(it, kind, n, off)
                    for which, (_, off, *_) in enumerate(LNS):
                        if slot == off % ITEMS and has(it, off):
                            normalise(which, batch(it, off))
                    if isinstance(it, int) and it == FIRST and 6 <= slot < 6 + NRAW - 2:
                        low_half(slot - 4)
                    if isinstance(it, int) and it == FIRST + 1 and slot == 0:
                        dve.wait_ge(s_split, NRAW)
                        for i, (_, lo) in enumerate((w1, w2, wh1, wh2)):
                            m = nc.vector.tensor_reduce(low_top[:, i:i + 1], lo[:].bitcast(F32), mybir.AxisListType.X,
                                                        ALU.max, apply_absolute_value=True)
                        m.then_inc(s_low, 1)

            def fill(it, kind, n, off):
                bb = batch(it, off)
                f = fill_bank(kind, n)
                src = ps_f[f][:]
                if kind in ("xt", "xt2"):
                    hi, lo = xt if kind == "xt" else xt2
                    dve.wait_ge(s_xhi if kind == "xt" else s_x2hi, count(bb, 1, 0))
                    tt(lo[:], src, hi[:].bitcast(F32), ALU.subtract).then_inc(s_xlo if kind == "xt" else s_x2lo, 1)
                elif kind == "kv":
                    g = n // 2
                    dve.wait_ge(s_kn, count(bb, 8, n))
                    if due(seen := count(bb, ITEMS, 4 * g + 3 - ITEMS)):
                        dve.wait_ge(s_o, seen)
                    v = src.rearrange("p (i k d) -> p i k d", i=2, k=2)
                    c = 2 * (n % 2)
                    tt(vn[:, g, c:c + 2, :], v[:, :, 1, :], kappa[:, c:c + 2].unsqueeze(2).to_broadcast([P, 2, P]),
                       ALU.mult).then_inc(s_vn, 1)
                elif kind == "up":
                    dve.wait_ge(s_up, count(bb, 4, n))
                    dve.wait_ge(s_silu, count(bb, 4, n))
                    if due(seen := count(bb, 8, n - 2)):
                        dve.wait_ge(s_hlo, seen)
                    nc.vector.scalar_tensor_tensor(out=pre[:, n % 2, :], in0=src, scalar=sc2[:, n:n + 1], in1=silu[:],
                                                   op0=ALU.mult, op1=ALU.mult).then_inc(s_h, 1)

            def low_half(n):
                _, stage, (hi, lo) = raw[n]
                dve.wait_ge(s_hi, n + 1)
                tt(lo[:], stage, hi[:].bitcast(F32), ALU.subtract).then_inc(s_split, 1)

            nc.vector.memset(ps_sk[:], 0.0)
            for n in range(2):
                low_half(n)
            dve.wait_ge(s_first, 16 * 2)
            runs(dve, body)

        @block.gpsimd
        def _(pool):
            tt = nc.gpsimd.tensor_tensor

            def root(which, bb):
                s, step = s_root[which], iter(range(ROOT_STEPS))
                v, y, z = mv[:, which, :, 1], rstd[:, which, :], newton[:, which, :]
                pool.wait_ge(s_ln[which], count(bb, 3, 1))

                def then(ins):
                    i = next(step)
                    ins.then_inc(s, 1)
                    if i < ROOT_STEPS - 1:
                        pool.wait_ge(s, count(bb, ROOT_STEPS, i))
                minus_half, three_halves, eps = (small[:, i, :] for i in range(3))
                then(tt(v, v, eps_t[:] if which == 1 else eps, ALU.add))
                then(tt(y, v, minus_half, ALU.pow))
                for _ in range(NEWTON):
                    then(tt(z, y, y, ALU.mult))
                    then(tt(z, z, v, ALU.mult))
                    then(tt(z, z, minus_half, ALU.mult))
                    then(tt(z, z, three_halves, ALU.add))
                    then(tt(y, y, z, ALU.mult))

            def body(it):
                for slot in range(ITEMS):
                    if isinstance(it, int) and it == FIRST and slot == PROJ % ITEMS:
                        pool.wait_ge(s_const, 16 * NCONST)
                    if isinstance(it, int) and it == FIRST + 1 and slot == 4:
                        pool.wait_ge(s_low, 1)
                        nc.gpsimd.tensor_reduce(flag[:], low_top[:], mybir.AxisListType.XYZWC, ALU.max).then_inc(s_flag, 1)
                    i0 = items(it, slot, 0)
                    if i0 and i0[3] < NC - 1:
                        bb, j, g, c = i0
                        u = 3 * g + c
                        pool.wait_ge(s_kn, count(bb, 8, 2 * g + c // 2))
                        if due(seen := count(bb, NU, u - 2)):
                            pool.wait_ge(s_sk, seen)
                        tt(kk[:, u % 2], kn[:, g, c, :].rearrange("p (h d) -> p h d", h=4).unsqueeze(2).to_broadcast([P, 4, 2, DK]),
                           kappa1[:, c, :].unsqueeze(1).unsqueeze(3).to_broadcast([P, 4, 2, DK]), ALU.mult).then_inc(s_kk, 1)
                    for which, off in enumerate((LN1, LN2A, LN2B, LN3)):
                        if slot == off % ITEMS and has(it, off):
                            root(which, batch(it, off))
                    if slot == LN2A % ITEMS and has(it, LN2A):
                        bb = batch(it, LN2A)
                        pool.wait_ge(s_ln[1], count(bb, 3, 2))
                        pool.wait_ge(s_xr, 16 * count(bb, 1, 0))
                        tt(x2[:], x2[:], xn2[:], ALU.add).then_inc(s_x2, 1)
                    if slot == LN3 % ITEMS and has(it, LN3):
                        bb = batch(it, LN3)
                        pool.wait_ge(s_ln[3], count(bb, 3, 2))
                        tt(outt, outt, x2_kept[:], ALU.add).then_inc(s_fin, 1)
                    if slot == KEEP % ITEMS and has(it, KEEP):
                        bb = batch(it, KEEP)
                        pool.wait_ge(s_x2, count(bb, 1, 0))
                        if due(seen := count(bb, 1, -1)):
                            pool.wait_ge(s_fin, seen)
                        tt(x2_kept[:], x2[:], small[:, 3, 0:1].unsqueeze(2).to_broadcast([P, NC, D]), ALU.mult).then_inc(s_res, 1)
                    for kind, n, off in fills(slot):
                        if kind == "left" and has(it, off):
                            bb = batch(it, off)
                            pool.wait_ge(s_leftc, count(bb, 8, n))
                            tt(right[:, n // 2, n % 2, :], right[:, n // 2, n % 2, :], rscale[:], ALU.mult).then_inc(s_rightc, 1)
                        if kind in ("up", "h1") and has(it, off):
                            bb = batch(it, off)
                            i = n + (4 if kind == "h1" else 0)
                            (hi, lo), made, used = (hid, s_h, s_h1) if kind == "up" else (gel, s_g1, s_h2)
                            hi, lo = (y[:, n * T:(n + 1) * T] for y in (hi, lo))
                            pool.wait_ge(made, count(bb, 4, n))
                            if due(seen := count(bb, 4, -1)):
                                pool.wait_ge(used, seen)
                            if due(seen := count(bb, 8, i - 8)):
                                pool.wait_ge(s_hlo, seen)
                            tt(hi, pre[:, n % 2, :], small[:, 3, 0:1].to_broadcast([P, T]), ALU.mult).then_inc(s_hhi, 1)
                            pool.wait_ge(s_hhi, count(bb, 8, i))
                            tt(lo, pre[:, n % 2, :], hi.bitcast(F32), ALU.subtract).then_inc(s_hlo, 1)

            pool.wait_ge(s_first, 16 * 2)
            runs(pool, body)


def kernel(**inputs):
    import concourse.bacc as bacc
    from concourse.bass_utils import run_bass_kernel_spmd

    a = {n.removeprefix("L0_"): np.asarray(v) for n, v in inputs.items()}
    wq, wk, wv = (a[f"attn_W{n}"].reshape(D, H, DK) for n in "qkv")
    arrays = {
        "x": a["attn_x"],
        "w_left": np.stack([wq, wk], 2).reshape(D, 8 * P),
        "w_kv": np.stack([wk.reshape(D, NG, P), wv.reshape(D, NG, P)], 2).reshape(D, 2 * 512),
        "w_o": a["attn_Wo"],
        "w_1": a["ffn_w1_w"].T, "w_2": a["ffn_w2_w"].T,
        "h_1": a["ffn_h1_w"].T.reshape(NM, P, HID).transpose(1, 0, 2).reshape(P, NM * HID),
        "h_2": a["ffn_h2_w"].T.reshape(NM, P, HID).transpose(1, 0, 2).reshape(P, NM * HID),
        "w_3": a["ffn_w3_w"].T,
        "f_1": a["ffn_w1_s"].reshape(NM, P).T, "f_2": a["ffn_w2_s"].reshape(NM, P).T,
        "f_h1": a["ffn_h1_s"].reshape(NM, P).T, "f_h2": a["ffn_h2_s"].reshape(NM, P).T,
        "f_3": np.broadcast_to(a["ffn_w3_s"][None, :], (P, D)),
    }
    arrays = {n: np.ascontiguousarray(v) for n, v in arrays.items()}
    names = list(arrays)
    arrays |= constants()

    nc = bacc.Bacc("TRN2", target_bir_lowering=False, num_devices=1)
    aps = {n: nc.dram_tensor(n, v.shape, F32, kind="ExternalInput").ap() for n, v in arrays.items()}
    out = nc.dram_tensor("out", (B, T, D), F32, kind="ExternalOutput").ap()
    build(nc, *[aps[n] for n in names], {n: v for n, v in aps.items() if n.startswith("c_")}, out)
    r = run_bass_kernel_spmd(nc, [arrays], core_ids=[0])
    return r.results[0]["out"]
```
